# Optimizing a Trainium2 kernel written in Bass

```python
import numpy as np
import jax
import jax.numpy as jnp

def _softmax(x, axis=-1):
    return jax.nn.softmax(x, axis=axis)

def _gelu(x):
    return jax.nn.gelu(x, approximate=True)

def _silu(x):
    return jax.nn.silu(x)

def _sigmoid(x):
    return jax.nn.sigmoid(x)

def _layernorm(x, axis=-1, eps=1e-05):
    m = jnp.mean(x, axis=axis, keepdims=True)
    v = jnp.var(x, axis=axis, keepdims=True)
    return (x - m) / jnp.sqrt(v + eps)

def _scatter_add(tgt, idx, src, axis=0):
    return tgt.at[idx].add(src)

def _segment_sum(src, seg, n):
    return jax.ops.segment_sum(src, seg, n)
kernel_name = 'mk_perceiver_d1_seqx_r8_d314b1'

def setup_inputs(seed: int=0):
    np.random.seed(seed)
    _w = jnp.asarray

    def _rec_inputs():
        import jax
        import jax.numpy as jnp
        _rk = jax.random.key(seed)
        x = -0.000125 + 0.9999 * jax.random.normal(jax.random.fold_in(_rk, 1), (16, 32, 512), jnp.float32)
        _lenS = 32 - jax.random.randint(jax.random.fold_in(_rk, 7), (16,), 0, max(1, 32 // 4) + 1, jnp.int32)
        _lenS2 = 512 - jax.random.randint(jax.random.fold_in(_rk, 8), (16,), 0, max(1, 512 // 4) + 1, jnp.int32)
        _ctx_4096P = jax.random.normal(jax.random.fold_in(_rk, 11), (16, 16, 512), jnp.float32)
        _ctx_4096c = jax.random.dirichlet(jax.random.fold_in(_rk, 511), 0.3 * jnp.ones((16,), jnp.float32), (16, 512))
        _ctx_4096t = jnp.einsum('bsk,bkd->bsd', _ctx_4096c, _ctx_4096P)
        _ctx_4096t = _ctx_4096t * jax.lax.rsqrt(jnp.mean(jnp.square(_ctx_4096t)) + 1e-12) * 0.953939
        ctx_4096 = -5.72187e-05 + 0.999849 * (_ctx_4096t + 0.3 * jax.random.normal(jax.random.fold_in(_rk, 611), (16, 512, 512), jnp.float32))
        return (x, ctx_4096)
    x, ctx_4096 = _rec_inputs()

    def _L0_xattn_setup():
        import jax, jax.numpy as jnp
        import numpy as np
        QMIN = 0.0
        QMAX = 255.0

        def fake_quant(x, scale, zp):
            s = scale.reshape(())
            z = zp.reshape(())
            q = jnp.clip(jnp.round(x / s + z), QMIN, QMAX)
            return (q - z) * s
        key = jax.random.key(seed)
        k1, k2 = jax.random.split(key)
        B, M, K, N = (4, 256, 512, 512)
        x1 = jax.random.normal(k1, (B, M, K), dtype=jnp.float32)
        x2 = jax.random.normal(k2, (B, K, N), dtype=jnp.float32)
        x1_scale = jnp.full((1,), 8.0 / 255.0, dtype=jnp.float32)
        x1_zp = jnp.full((1,), 128.0, dtype=jnp.float32)
        x2_scale = jnp.full((1,), 8.0 / 255.0, dtype=jnp.float32)
        x2_zp = jnp.full((1,), 128.0, dtype=jnp.float32)
        return {'x1': x1, 'x2': x2, 'x1_scale': x1_scale, 'x1_zp': x1_zp, 'x2_scale': x2_scale, 'x2_zp': x2_zp}
    _L0_xattn_all = _L0_xattn_setup()
    _L0_xattn_in = {k: v for k, v in _L0_xattn_all.items() if k in ('x1_scale', 'x1_zp', 'x2_scale', 'x2_zp')}
    del _L0_xattn_all

    def _L0_attn_setup():
        import jax, jax.numpy as jnp
        import numpy as np
        HIDDEN = 512
        NUM_HEADS = 32
        HEAD_DIM = HIDDEN // NUM_HEADS

        def _fp8_roundtrip(x):
            return x.astype(jnp.float8_e4m3fn).astype(jnp.float32)
        key = jax.random.key(seed)
        ks = jax.random.split(key, 10)
        B, S = (2, 512)
        hidden_states = jax.random.normal(ks[0], (B, S, HIDDEN), dtype=jnp.float32)
        scale = 0.02

        def lin(kw, kb):
            w = jax.random.normal(kw, (HIDDEN, HIDDEN), dtype=jnp.float32) * scale
            b = jax.random.normal(kb, (HIDDEN,), dtype=jnp.float32) * scale
            return (w, b)
        wq, bq = lin(ks[1], ks[2])
        wk, bk = lin(ks[3], ks[4])
        wv, bv = lin(ks[5], ks[6])
        wl, bl = lin(ks[7], ks[8])
        wq, bq = (_fp8_roundtrip(wq), _fp8_roundtrip(bq))
        wk, bk = (_fp8_roundtrip(wk), _fp8_roundtrip(bk))
        wv, bv = (_fp8_roundtrip(wv), _fp8_roundtrip(bv))
        return {'hidden_states': hidden_states, 'wq': wq, 'bq': bq, 'wk': wk, 'bk': bk, 'wv': wv, 'bv': bv, 'wl': wl, 'bl': bl}
    _L0_attn_all = _L0_attn_setup()
    _L0_attn_in = {k: v for k, v in _L0_attn_all.items() if k in ('wq', 'bq', 'wk', 'bk', 'wv', 'bv', 'wl', 'bl')}
    del _L0_attn_all

    def _L0_ffn_setup():
        import jax, jax.numpy as jnp
        import numpy as np
        IN_F = 512
        OUT_F = 512
        RANK = 8
        NUM_EXPERTS = 64
        TOP_K = 16
        ROUTER_DIM = 16
        ALPHA = 32
        SCALING = ALPHA / TOP_K
        BOTTLENECK = NUM_EXPERTS * RANK
        key = jax.random.key(seed)
        ks = jax.random.split(key, 5)
        x = jax.random.normal(ks[0], (4, 512, IN_F), dtype=jnp.float32)
        bound_a = float(np.sqrt(6.0 / IN_F))
        A_w = jax.random.uniform(ks[1], (BOTTLENECK, IN_F), jnp.float32, -bound_a, bound_a)
        B_w = jax.random.normal(ks[2], (OUT_F, BOTTLENECK), dtype=jnp.float32) * 0.02
        Wq_w = jax.random.normal(ks[3], (ROUTER_DIM, IN_F), dtype=jnp.float32) * 0.02
        keys = jax.random.normal(ks[4], (NUM_EXPERTS, ROUTER_DIM), dtype=jnp.float32) * 0.01
        return {'x': x, 'A_w': A_w, 'B_w': B_w, 'Wq_w': Wq_w, 'keys': keys}
    _L0_ffn_all = _L0_ffn_setup()
    _L0_ffn_in = {k: v for k, v in _L0_ffn_all.items() if k in ('A_w', 'B_w', 'Wq_w', 'keys')}
    del _L0_ffn_all
    return {'x': x, 'ctx_4096': ctx_4096, 'L0_xattn_x1_scale': _L0_xattn_in['x1_scale'], 'L0_xattn_x1_zp': _L0_xattn_in['x1_zp'], 'L0_xattn_x2_scale': _L0_xattn_in['x2_scale'], 'L0_xattn_x2_zp': _L0_xattn_in['x2_zp'], 'L0_attn_wq': _L0_attn_in['wq'], 'L0_attn_bq': _L0_attn_in['bq'], 'L0_attn_wk': _L0_attn_in['wk'], 'L0_attn_bk': _L0_attn_in['bk'], 'L0_attn_wv': _L0_attn_in['wv'], 'L0_attn_bv': _L0_attn_in['bv'], 'L0_attn_wl': _L0_attn_in['wl'], 'L0_attn_bl': _L0_attn_in['bl'], 'L0_ffn_A_w': _L0_ffn_in['A_w'], 'L0_ffn_B_w': _L0_ffn_in['B_w'], 'L0_ffn_Wq_w': _L0_ffn_in['Wq_w'], 'L0_ffn_keys': _L0_ffn_in['keys']}

def reference(x, ctx_4096, L0_xattn_x1_scale, L0_xattn_x1_zp, L0_xattn_x2_scale, L0_xattn_x2_zp, L0_attn_wq, L0_attn_bq, L0_attn_wk, L0_attn_bk, L0_attn_wv, L0_attn_bv, L0_attn_wl, L0_attn_bl, L0_ffn_A_w, L0_ffn_B_w, L0_ffn_Wq_w, L0_ffn_keys):
    import jax
    import jax.numpy as jnp

    def _L0_xattn_ref(x1, x2, x1_scale, x1_zp, x2_scale, x2_zp):
        import jax, jax.numpy as jnp
        import numpy as np
        QMIN = 0.0
        QMAX = 255.0

        def fake_quant(x, scale, zp):
            s = scale.reshape(())
            z = zp.reshape(())
            q = jnp.clip(jnp.round(x / s + z), QMIN, QMAX)
            return (q - z) * s
        q1 = fake_quant(x1, x1_scale, x1_zp)
        q2 = fake_quant(x2, x2_scale, x2_zp)
        return jnp.matmul(q1, q2)

    def _L0_attn_ref(hidden_states, wq, bq, wk, bk, wv, bv, wl, bl):
        import jax, jax.numpy as jnp
        import numpy as np
        HIDDEN = 512
        NUM_HEADS = 32
        HEAD_DIM = HIDDEN // NUM_HEADS

        def _fp8_roundtrip(x):
            return x.astype(jnp.float8_e4m3fn).astype(jnp.float32)
        B, S, E = hidden_states.shape
        H, D = (NUM_HEADS, HEAD_DIM)
        q = (hidden_states @ wq.T + bq).reshape(B, S, H, D)
        k = (hidden_states @ wk.T + bk).reshape(B, S, H, D)
        v = (hidden_states @ wv.T + bv).reshape(B, S, H, D)
        latent = hidden_states @ wl.T + bl
        scores = jnp.einsum('bshd,bstd->bsht', q, k) / np.sqrt(D).astype(np.float32)
        probs = jax.nn.softmax(scores, axis=-1)
        context = jnp.einsum('bsht,bstd->bshd', probs, v).reshape(B, S, E)
        return context

    def _L0_ffn_ref(x, A_w, B_w, Wq_w, keys):
        import jax, jax.numpy as jnp
        import numpy as np
        IN_F = 512
        OUT_F = 512
        RANK = 8
        NUM_EXPERTS = 64
        TOP_K = 16
        ROUTER_DIM = 16
        ALPHA = 32
        SCALING = ALPHA / TOP_K
        BOTTLENECK = NUM_EXPERTS * RANK
        q = jnp.einsum('bsd,rd->bsr', x, Wq_w)
        scores = jnp.einsum('bsr,er->bse', q, keys)
        top_vals, top_idx = jax.lax.top_k(scores, TOP_K)
        top_w = jax.nn.softmax(top_vals, axis=-1)
        gate = jnp.sum(jax.nn.one_hot(top_idx, NUM_EXPERTS, dtype=top_w.dtype) * top_w[..., None], axis=-2)
        z = jnp.einsum('bsd,nd->bsn', x, A_w)
        z = z.reshape(*z.shape[:-1], NUM_EXPERTS, RANK)
        z_gated = (z * gate[..., None]).reshape(*z.shape[:-2], BOTTLENECK)
        out = jnp.einsum('bsn,on->bso', z_gated, B_w) * SCALING
        return out
    x = x + _L0_xattn_ref(_layernorm(x, axis=-1), ctx_4096, L0_xattn_x1_scale, L0_xattn_x1_zp, L0_xattn_x2_scale, L0_xattn_x2_zp)
    x = x + _L0_attn_ref(_layernorm(x, axis=-1), L0_attn_wq, L0_attn_bq, L0_attn_wk, L0_attn_bk, L0_attn_wv, L0_attn_bv, L0_attn_wl, L0_attn_bl)
    x = x + _L0_ffn_ref(_layernorm(x, axis=-1), L0_ffn_A_w, L0_ffn_B_w, L0_ffn_Wq_w, L0_ffn_keys)
    return x

_drawn_inputs = setup_inputs


def setup_inputs(seed=0):
    import zlib

    import numpy as np

    out = dict(_drawn_inputs(seed))
    spreads = {}
    factors = {'L0_attn_wq': 8.0,
     'L0_attn_bq': 8.0,
     'L0_attn_wk': 8.0,
     'L0_attn_bk': 8.0,
     'L0_attn_wv': 8.0,
     'L0_attn_bv': 46.556,
     'L0_ffn_A_w': 8.0,
     'L0_ffn_B_w': 8.0,
     'L0_ffn_Wq_w': 8.0,
     'L0_ffn_keys': 8.0}
    for name, (base, spread) in spreads.items():
        noise = np.random.default_rng([zlib.crc32(name.encode()), seed]).standard_normal(out[name].shape)
        drawn = base * np.exp(spread * noise) if base else spread * noise
        out[name] = jnp.asarray(drawn.astype(out[name].dtype))
    for name, factor in factors.items():
        out[name] = (out[name] * factor).astype(out[name].dtype)
    return out
```

```python
from contextlib import ExitStack

import concourse.bass as bass
from concourse import mybir

ALU = mybir.AluOpType
ACT = mybir.ActivationFunctionType
AX_X = mybir.AxisListType.X
F32 = mybir.dt.float32
BF16 = mybir.dt.bfloat16
U8 = mybir.dt.uint8

P = 128
Q = 32
LN_EPS = 1e-5
QMAX = 255.0
CENTER = 128.0
NEG = -3.0e38
TOP_K = 16
SCALING = 2.0

RAW_SLOTS = 3
U8_SLOTS = 4
BF_SLOTS = 4



def view(ap, offset, dims):
    return bass.AP(ap.tensor, ap.offset + offset, [ap.ap[0]] + dims)


def build(nc, x, ctx, x1_scale, x1_zp, x2_scale, x2_zp, wqT, bq, wkT, bk, wvT, bv, aT, bT, wrT, keysT, out):
    NB, L, D = x.shape
    TILES = NB * L // P
    BPT = P // L
    KC = D // P
    E, RD = keysT.shape[1], keysT.shape[0]
    RANK = aT.shape[1] // E
    H = 32
    HD = D // H
    LW = L + 1
    assert L == Q and H == Q and HD == 16 and ctx.shape == (NB, D, D)

    with ExitStack() as stack:
        def sb(name, shape, dt=F32):
            return stack.enter_context(nc.sbuf_tensor(name, shape, dt))

        def ps(name, shape, dt=F32):
            return stack.enter_context(nc.psum_tensor(name, shape, dt))

        def sem(name):
            return stack.enter_context(nc.semaphore(name))

        sem_x_in = sem("x_in")
        sem_scalars_in = sem("scalars_in")
        sem_biases_in = sem("biases_in")
        sem_wq_in = sem("wq_in")
        sem_wk_in = sem("wk_in")
        sem_wv_in = sem("wv_in")
        sem_a_in = sem("a_in")
        sem_b_in = sem("b_in")
        sem_router_in = sem("router_in")
        sem_y_out0 = sem("y_out0")
        sem_y_out1 = sem("y_out1")
        sem_zeros = sem("zeros")
        sem_identity_mask = sem("identity_mask")
        sem_identity = sem("identity")
        sem_identity_bf = sem("identity_bf")
        sem_ones_q1 = sem("ones_q1")
        sem_v_ones = sem("v_ones")
        sem_q_zeros = sem("q_zeros")
        sem_tails = sem("tails")
        sem_recip = sem("recip")
        sem_consts = sem("consts")
        sem_row_scale = sem("row_scale")
        sem_ln1_stats = sem("ln1_stats")
        sem_ln1_mean = sem("ln1_mean")
        sem_ln1_eps = sem("ln1_eps")
        sem_ln1_rstd = sem("ln1_rstd")
        sem_ln1_done = sem("ln1_done")
        sem_x_u8 = sem("x_u8")
        sem_q1_ready = sem("q1_ready")
        sem_q1_sum = sem("q1_sum")
        sem_q1_base = sem("q1_base")
        sem_q1_transposed = sem("q1_transposed")
        sem_q1T_ready = sem("q1T_ready")
        sem_x_shifted = sem("x_shifted")
        sem_ctx_u8 = sem("ctx_u8")
        sem_ctx_bf = sem("ctx_bf")
        sem_stage1_done = sem("stage1_done")
        sem_colsum_scaled = sem("colsum_scaled")
        sem_y1_ready = sem("y1_ready")
        sem_y1_transposed = sem("y1_transposed")
        sem_x1_ready = sem("x1_ready")
        sem_ln2_stats = sem("ln2_stats")
        sem_ln2_mean = sem("ln2_mean")
        sem_ln2_eps = sem("ln2_eps")
        sem_ln2_rstd = sem("ln2_rstd")
        sem_h2_ready = sem("h2_ready")
        sem_h2_transposed = sem("h2_transposed")
        sem_h2T_ready = sem("h2T_ready")
        sem_q_done = sem("q_done")
        sem_k_done = sem("k_done")
        sem_v_done = sem("v_done")
        sem_q_biased = sem("q_biased")
        sem_k_biased = sem("k_biased")
        sem_v_biased = sem("v_biased")
        sem_qT_ready = sem("qT_ready")
        sem_q_diag = sem("q_diag")
        sem_kT_ready = sem("kT_ready")
        sem_v_diag = sem("v_diag")
        sem_scores_done = sem("scores_done")
        sem_s_max = sem("s_max")
        sem_s_shifted = sem("s_shifted")
        sem_s_exp = sem("s_exp")
        sem_eT_ready = sem("eT_ready")
        sem_context_done = sem("context_done")
        sem_oT_ready = sem("oT_ready")
        sem_o_recip = sem("o_recip")
        sem_o_scaled = sem("o_scaled")
        sem_x2_ready = sem("x2_ready")
        sem_ln3_stats = sem("ln3_stats")
        sem_ln3_mean = sem("ln3_mean")
        sem_ln3_eps = sem("ln3_eps")
        sem_ln3_rstd = sem("ln3_rstd")
        sem_h3_ready = sem("h3_ready")
        sem_h3_transposed = sem("h3_transposed")
        sem_h3T_ready = sem("h3T_ready")
        sem_router_q_done = sem("router_q_done")
        sem_router_q_ready = sem("router_q_ready")
        sem_router_done = sem("router_done")
        sem_r_copied = sem("r_copied")
        sem_r_top8 = sem("r_top8")
        sem_r_first8 = sem("r_first8")
        sem_r_next8 = sem("r_next8")
        sem_r_masked = sem("r_masked")
        sem_r_negmax = sem("r_negmax")
        sem_r_exp = sem("r_exp")
        sem_gate_ready = sem("gate_ready")
        sem_gate_sum = sem("gate_sum")
        sem_gate_recip = sem("gate_recip")
        sem_z_done = sem("z_done")
        sem_z_gated = sem("z_gated")
        sem_zg_transposed = sem("zg_transposed")
        sem_zgT_ready = sem("zgT_ready")
        sem_out_done = sem("out_done")
        sem_y_ready = sem("y_ready")
        ctx_in = [sem(f"ctx_in{i}") for i in range(RAW_SLOTS)]

        wq, wk, wv, wa, wb = (sb(n, [P, KC, D]) for n in ("wq", "wk", "wv", "wa", "wb"))
        wr = sb("wr", [P, KC, RD])
        keys = sb("keys", [RD, E])
        bias_q, bias_k, bias_v = (sb(n, [P, D]) for n in ("bias_q", "bias_k", "bias_v"))
        ident = sb("ident", [P, P])
        ident_bf = sb("ident_bf", [P, P], BF16)
        sc_in = sb("sc_in", [P, 4])
        sc_recip = sb("sc_recip", [P, 4])
        sc_off = sb("sc_off", [P, 2])
        sc_prod = sb("sc_prod", [P, 1])
        sc_row = sb("sc_row", [P, 1])
        sc_base = sb("sc_base", [P, 1])
        minus_half = sb("minus_half", [P, 1])
        x_sb = sb("x_sb", [P, TILES, D])
        h1 = sb("h1", [P, 2, D])
        h1_u8 = sb("h1_u8", [P, 2, D], U8)
        q1 = sb("q1", [P, 2, D], BF16)
        q1_rowsum = sb("q1_rowsum", [P, TILES])
        row_term = sb("row_term", [P, TILES])
        q1T = sb("q1T", [P, TILES, KC, BPT, LW], BF16)
        raw = sb("raw", [P, RAW_SLOTS, KC * D])
        cu8 = sb("cu8", [P, U8_SLOTS, KC * D], U8)
        cbf = sb("cbf", [P, BF_SLOTS, KC, D], BF16)
        colsum = sb("colsum", [P, KC * BPT])
        y1T = sb("y1T", [P, KC, P])
        x1 = sb("x1", [P, 2, D])
        stats = sb("stats", [P, 3, TILES, 6])
        mean_var = sb("mean_var", [P, 3, TILES, 2])
        var_eps = sb("var_eps", [P, 3, TILES])
        rstd = sb("rstd", [P, 3, TILES])
        h2 = sb("h2", [P, D])
        h2T = sb("h2T", [P, KC, P])
        q_sb, k_sb = (sb(n, [P, D + HD]) for n in ("q_sb", "k_sb"))
        v_sb = sb("v_sb", [P, D])
        qT = sb("qT", [P, Q, H])
        kT = sb("kT", [P, Q, H])
        qdiag = sb("qdiag", [P, Q, P])
        vdiag = sb("vdiag", [P, Q, P])
        s_max = sb("s_max", [P, Q])
        probs = sb("probs", [P, Q, H])
        eT = sb("eT", [P, Q, H])
        oT = sb("oT", [P, H, Q])
        o_recip = sb("o_recip", [P, H])
        attn = sb("attn", [P, D])
        x2 = sb("x2", [P, 2, D])
        h3 = sb("h3", [P, D])
        h3T = sb("h3T", [P, KC, P])
        router_qT = sb("router_qT", [RD, P])
        r_scores = sb("r_scores", [P, 2, E])
        r_rest = sb("r_rest", [P, E])
        r_top = sb("r_top", [P, 2, 8])
        r_negmax = sb("r_negmax", [P, 1])
        r_exp = sb("r_exp", [P, 2, E])
        gate = sb("gate", [P, E])
        gate_sum = sb("gate_sum", [P, 1])
        gate_recip = sb("gate_recip", [P, 1])
        zg = sb("zg", [P, D])
        zgT = sb("zgT", [P, KC, P])
        y = sb("y", [P, 2, D])

        ps1 = ps("ps1", [P, 2, 512])
        ps_att = ps("ps_att", [P, Q, H])
        ps_a = ps("ps_a", [P, D])
        ps_b = ps("ps_b", [P, D])
        ps_t0 = ps("ps_t0", [P, 512])
        ps_t1 = ps("ps_t1", [P, 512])
        ps_t = [ps_t0, ps_t1]

        PW = 2 * BPT * LW
        x_dram = x.rearrange("b l d -> (b l) d").rearrange("(t p) d -> p t d", p=P)
        out_dram = out.rearrange("b l d -> (b l) d").rearrange("(t p) d -> p t d", p=P)
        ctx_dram = ctx.rearrange("n (p c) d -> n p (c d)", c=KC)
        chunked = lambda w: w.rearrange("(c p) n -> p c n", p=P)

        block = stack.enter_context(nc.Block())

        @block.sync
        def _(sp):
            def load_ctx(n):
                if n >= RAW_SLOTS:
                    sp.wait_ge(sem_ctx_u8, n - RAW_SLOTS + 1)
                sp.dma_start(raw[:, n % RAW_SLOTS, :], ctx_dram[n]).then_inc(ctx_in[n % RAW_SLOTS], 16)

            for c, v in enumerate((x1_scale, x1_zp, x2_scale, x2_zp)):
                sp.dma_start(sc_in[:, c:c + 1], v.partition_broadcast(P)).then_inc(sem_scalars_in, 16)
            sp.dma_start(x_sb[:, :, :], x_dram).then_inc(sem_x_in, 16)
            for n in range(BPT):
                load_ctx(n)
            sp.dma_start(wq[:, :, :], chunked(wqT)).then_inc(sem_wq_in, 16)
            for t, v in ((bias_q, bq), (bias_k, bk), (bias_v, bv)):
                sp.dma_start(t[:, :], v.partition_broadcast(P)).then_inc(sem_biases_in, 16)
            sp.dma_start(wk[:, :, :], chunked(wkT)).then_inc(sem_wk_in, 16)
            sp.dma_start(wv[:, :, :], chunked(wvT)).then_inc(sem_wv_in, 16)
            for n in range(BPT, BPT + 2):
                load_ctx(n)
            sp.dma_start(wr[:, :, :], chunked(wrT)).then_inc(sem_router_in, 16)
            sp.dma_start(keys[:, :], keysT).then_inc(sem_router_in, 16)
            sp.dma_start(wa[:, :, :], chunked(aT)).then_inc(sem_a_in, 16)
            sp.dma_start(wb[:, :, :], chunked(bT)).then_inc(sem_b_in, 16)
            for n in range(BPT + 2, NB):
                load_ctx(n)
            for t in range(TILES):
                sp.wait_ge(sem_y_ready, t + 1)
                sp.dma_start(out_dram[:, t, :], y[:, t % 2, :]).then_inc((sem_y_out0, sem_y_out1)[t % 2], 16)
            sp.wait_ge(sem_y_out0, 16 * ((TILES + 1) // 2))
            sp.wait_ge(sem_y_out1, 16 * (TILES // 2))

        @block.gpsimd
        def _(pool):
            nc.gpsimd.memset(ident[:, :], 0.0).then_inc(sem_identity_mask, 1)
            pool.wait_ge(sem_identity_mask, 1)
            nc.gpsimd.affine_select(out=ident[:, :], in_=ident[:, :], compare_op=ALU.not_equal, fill=1.0, base=0,
                                    pattern=[[-1, P]], channel_multiplier=1).then_inc(sem_identity, 1)
            nc.gpsimd.memset(minus_half[:, :], -0.5).then_inc(sem_identity_mask, 1)
            pool.wait_ge(sem_identity, 1)
            nc.gpsimd.tensor_copy(ident_bf[:, :], ident[:, :]).then_inc(sem_identity_bf, 1)
            pool.wait_ge(sem_identity_mask, 2)
            nc.gpsimd.memset(q1T[:, :, :, :, L:LW], 1.0).then_inc(sem_ones_q1, 1)
            nc.gpsimd.memset(k_sb[:, D:], 0.0).then_inc(sem_tails, 1)
            nc.gpsimd.memset(q_sb[:, D:], 0.0).then_inc(sem_tails, 1)

            def rsqrt(norm, t, mean_sem, eps_sem, rstd_sem):
                pool.wait_ge(mean_sem, t + 1)
                nc.gpsimd.tensor_scalar(var_eps[:, norm, t:t + 1], mean_var[:, norm, t, 1:2], LN_EPS, None,
                                        ALU.add).then_inc(eps_sem, 1)
                pool.wait_ge(eps_sem, t + 1)
                nc.gpsimd.tensor_tensor(rstd[:, norm, t:t + 1], var_eps[:, norm, t:t + 1], minus_half[:, :],
                                        ALU.pow).then_inc(rstd_sem, 1)

            for t in range(TILES):
                rsqrt(0, t, sem_ln1_mean, sem_ln1_eps, sem_ln1_rstd)
            nc.gpsimd.memset(qdiag[:, :, :], 0.0).then_inc(sem_q_zeros, 1)
            nc.gpsimd.memset(vdiag[:, :, :], 0.0).then_inc(sem_zeros, 1)
            pool.wait_ge(sem_zeros, 1)
            for j in range(BPT):
                nc.gpsimd.memset(vdiag[Q * j:Q * j + Q, :, Q * j + HD:Q * j + HD + 1], 1.0).then_inc(sem_v_ones, 1)
                pool.wait_ge(sem_v_ones, j + 1)
            rsqrt(1, 0, sem_ln2_mean, sem_ln2_eps, sem_ln2_rstd)
            for t in range(TILES):
                if t + 1 < TILES:
                    rsqrt(1, t + 1, sem_ln2_mean, sem_ln2_eps, sem_ln2_rstd)
                rsqrt(2, t, sem_ln3_mean, sem_ln3_eps, sem_ln3_rstd)

        @block.scalar
        def _(act):
            def quantise_x(t):
                act.wait_ge(sem_ln1_done, t + 1)
                if t == 0:
                    act.wait_ge(sem_recip, 1)
                if t >= 2:
                    act.wait_ge(sem_q1_ready, t - 1)
                nc.scalar.activation(h1_u8[:, t % 2, :], h1[:, t % 2, :], ACT.Identity, bias=sc_in[:, 1:2],
                                     scale=sc_recip[:, 0:1]).then_inc(sem_x_u8, 1)

            def quantise_ctx(n):
                if n >= NB:
                    return
                act.wait_ge(ctx_in[n % RAW_SLOTS], 16 * (n // RAW_SLOTS + 1))
                if n >= U8_SLOTS:
                    act.wait_ge(sem_ctx_bf, n - U8_SLOTS + 1)
                nc.scalar.activation(cu8[:, n % U8_SLOTS, :], raw[:, n % RAW_SLOTS, :], ACT.Identity,
                                     bias=sc_in[:, 3:4], scale=sc_recip[:, 2:3]).then_inc(sem_ctx_u8, 1)

            def copy_h2T(t):
                act.wait_ge(sem_h2_transposed, t + 1)
                if t >= 1:
                    act.wait_ge(sem_v_done, t)
                nc.scalar.copy(h2T[:, :, :], ps_t1[:, :]).then_inc(sem_h2T_ready, 1)

            def diagonal_q(t):
                act.wait_ge(sem_qT_ready, t + 1)
                if t == 0:
                    act.wait_ge(sem_q_zeros, 1)
                if t >= 1:
                    act.wait_ge(sem_scores_done, t)
                for j in range(BPT):
                    nc.scalar.copy(qdiag[Q * j:Q * j + HD, :, Q * j:Q * j + Q],
                                   qT[Q * j:Q * j + HD, :, :]).then_inc(sem_q_diag, 1)

            def exp_scores(t):
                act.wait_ge(sem_s_shifted, t + 1)
                nc.scalar.activation(probs[:, :, :], probs[:, :, :], ACT.Exp, scale=HD ** -0.5).then_inc(sem_s_exp, 1)

            def copy_h3T(t):
                act.wait_ge(sem_h3_transposed, t + 1)
                if t >= 1:
                    act.wait_ge(sem_z_done, t)
                nc.scalar.copy(h3T[:, :, :], ps_t1[:, :]).then_inc(sem_h3T_ready, 1)

            def router(t):
                act.wait_ge(sem_router_q_done, t + 1)
                if t >= 1:
                    act.wait_ge(sem_router_done, t)
                nc.scalar.copy(router_qT[:, :], ps_t0[0:RD, 0:P]).then_inc(sem_router_q_ready, 1)
                act.wait_ge(sem_r_masked, t + 1)
                act.wait_ge(sem_r_negmax, t + 1)
                if t >= 1:
                    act.wait_ge(sem_gate_ready, t)
                nc.scalar.activation(r_exp[:, :, :], r_scores[:, :, :], ACT.Exp,
                                     bias=r_negmax[:, 0:1]).then_inc(sem_r_exp, 1)

            def copy_zgT(t):
                act.wait_ge(sem_zg_transposed, t + 1)
                if t >= 1:
                    act.wait_ge(sem_out_done, t)
                nc.scalar.copy(zgT[:, :, :], ps_t1[:, :]).then_inc(sem_zgT_ready, 1)

            for t in range(TILES):
                quantise_x(t)
            for n in range(BPT):
                quantise_ctx(n)
            copy_h2T(0)
            quantise_ctx(BPT)
            quantise_ctx(BPT + 1)
            for t in range(TILES + 1):
                if t < TILES:
                    quantise_ctx(BPT * (t + 1) + 2)
                    quantise_ctx(BPT * (t + 1) + 3)
                    diagonal_q(t)
                if t >= 1:
                    copy_h3T(t - 1)
                    router(t - 1)
                if t < TILES:
                    exp_scores(t)
                if t >= 1:
                    copy_zgT(t - 1)
                if t < TILES:
                    quantise_ctx(BPT * (t + 2))
                    quantise_ctx(BPT * (t + 2) + 1)
                if t + 1 < TILES:
                    copy_h2T(t + 1)

        @block.vector
        def _(dve):
            def norm_stats(src, norm, t, stats_sem, mean_sem):
                nc.vector.bn_stats(stats[:, norm, t, :], src).then_inc(stats_sem, 1)
                dve.wait_ge(stats_sem, t + 1)
                nc.vector.bn_aggr(mean_var[:, norm, t, :], stats[:, norm, t, :]).then_inc(mean_sem, 1)

            def norm_apply(dst, src, norm, t, rstd_sem, done_sem):
                dve.wait_ge(rstd_sem, t + 1)
                nc.vector.tensor_scalar(dst, src, mean_var[:, norm, t, 0:1], rstd[:, norm, t:t + 1],
                                        ALU.subtract, ALU.mult).then_inc(done_sem, 1)

            def scalars():
                dve.wait_ge(sem_scalars_in, 64)
                nc.vector.reciprocal(sc_recip[:, :], sc_in[:, :]).then_inc(sem_recip, 1)
                nc.vector.tensor_scalar(sc_off[:, :], sc_in[:, 1:4:2], -1.0, CENTER,
                                        ALU.mult, ALU.add).then_inc(sem_consts, 1)
                nc.vector.tensor_tensor(sc_prod[:, :], sc_in[:, 0:1], sc_in[:, 2:3], ALU.mult).then_inc(sem_consts, 1)
                dve.wait_ge(sem_consts, 2)
                nc.vector.tensor_tensor(sc_row[:, :], sc_off[:, 1:2], sc_prod[:, :], ALU.mult).then_inc(sem_consts, 1)
                nc.vector.tensor_scalar(sc_base[:, :], sc_off[:, 0:1], float(D), None,
                                        ALU.mult).then_inc(sem_consts, 1)

            def center_q1(t):
                dve.wait_ge(sem_x_u8, t + 1)
                if t >= 2:
                    dve.wait_ge(sem_q1_transposed, t - 1)
                nc.vector.tensor_scalar(q1[:, t % 2, :], h1_u8[:, t % 2, :], CENTER, None, ALU.subtract, ALU.add,
                                        accum_out=q1_rowsum[:, t:t + 1]).then_inc(sem_q1_ready, 1)

            def copy_q1T(t):
                dve.wait_ge(sem_q1_transposed, t + 1)
                if t == 0:
                    dve.wait_ge(sem_ones_q1, 1)
                src = ps_t[t % 2][:, 0:D // 2].bitcast(BF16).rearrange("p (c b l) -> p c b l", c=KC, l=L)
                nc.vector.tensor_copy(q1T[:, t, :, :, 0:L], src).then_inc(sem_q1T_ready, 1)

            def center_ctx(n):
                if n >= NB:
                    return
                dve.wait_ge(sem_ctx_u8, n + 1)
                if n >= BF_SLOTS:
                    dve.wait_ge(sem_stage1_done, n - BF_SLOTS + 1)
                nc.vector.tensor_scalar(cbf[:, n % BF_SLOTS, :, :], cu8[:, n % U8_SLOTS, :], CENTER, None,
                                        ALU.subtract).then_inc(sem_ctx_bf, 1)

            def finish_product(t):
                dve.wait_ge(sem_stage1_done, BPT * (t + 1))
                ones_col = view(ps1[:, 0, :], L, [[512, 2], [LW, 2 * BPT]])
                nc.vector.tensor_scalar(colsum[:, :].rearrange("p (k g) -> p k g", k=2), ones_col, sc_off[:, 0:1],
                                        None, ALU.mult).then_inc(sem_colsum_scaled, 1)
                dve.wait_ge(sem_colsum_scaled, t + 1)
                if t >= 1:
                    dve.wait_ge(sem_y1_transposed, t)
                for k in range(2):
                    G = 2 * BPT
                    nc.vector.tensor_tensor(
                        y1T[:, 2 * k:2 * k + 2, :].rearrange("p c n -> p (c n)").rearrange("p (g l) -> p g l", l=L),
                        view(ps1[:, k, :], 0, [[LW, G], [1, L]]),
                        view(colsum[:, :], G * k, [[1, G], [0, L]]), ALU.add).then_inc(sem_y1_ready, 1)

            def residual_1(t):
                dve.wait_ge(sem_y1_transposed, t + 1)
                nc.vector.scalar_tensor_tensor(out=x1[:, t % 2, :], in0=ps_t0[:, :], scalar=sc_prod[:, 0:1],
                                               in1=x_sb[:, t, :], op0=ALU.mult, op1=ALU.add).then_inc(sem_x1_ready, 1)
                dve.wait_ge(sem_x1_ready, t + 1)
                norm_stats(x1[:, t % 2, :], 1, t, sem_ln2_stats, sem_ln2_mean)

            def norm_2(t):
                if t >= 1:
                    dve.wait_ge(sem_h2_transposed, t)
                norm_apply(h2[:, :], x1[:, t % 2, :], 1, t, sem_ln2_rstd, sem_h2_ready)

            def head_windows(ap):
                return view(ap, 0, [[HD, H], [1, Q]])

            def q_to_heads(t):
                dve.wait_ge(sem_q_done, t + 1)
                if t == 0:
                    dve.wait_ge(sem_biases_in, 48)
                    dve.wait_ge(sem_tails, 2)
                nc.vector.tensor_tensor(q_sb[:, 0:D], ps_a[:, :], bias_q[:, :], ALU.add).then_inc(sem_q_biased, 1)
                dve.wait_ge(sem_q_biased, t + 1)
                if t >= 1:
                    dve.wait_ge(sem_q_diag, BPT * t)
                nc.vector.transpose(view(qT[:, 0, :], 0, [[1, H], [H, Q]]),
                                    head_windows(q_sb[:, :])).then_inc(sem_qT_ready, 1)

            def k_to_heads(t):
                dve.wait_ge(sem_k_done, t + 1)
                nc.vector.tensor_tensor(k_sb[:, 0:D], ps_b[:, :], bias_k[:, :], ALU.add).then_inc(sem_k_biased, 1)
                dve.wait_ge(sem_k_biased, t + 1)
                if t >= 1:
                    dve.wait_ge(sem_scores_done, t)
                nc.vector.transpose(view(kT[:, 0, :], 0, [[1, H], [H, Q]]),
                                    head_windows(k_sb[:, :])).then_inc(sem_kT_ready, 1)

            def v_to_heads(t):
                dve.wait_ge(sem_v_done, t + 1)
                nc.vector.tensor_tensor(v_sb[:, :], ps_a[:, :], bias_v[:, :], ALU.add).then_inc(sem_v_biased, 1)
                dve.wait_ge(sem_v_biased, t + 1)
                if t == 0:
                    dve.wait_ge(sem_v_ones, BPT)
                if t >= 1:
                    dve.wait_ge(sem_context_done, t)
                for j in range(BPT):
                    rows = slice(Q * j, Q * j + Q)
                    nc.vector.transpose(view(vdiag[rows, 0, :], Q * j, [[1, HD], [P, Q]]),
                                        view(v_sb[rows, :], 0, [[1, HD], [HD, H]])).then_inc(sem_v_diag, 1)

            def softmax_shift(t):
                dve.wait_ge(sem_scores_done, t + 1)
                nc.vector.tensor_reduce(s_max[:, :], ps_att[:, :, :], AX_X, ALU.max).then_inc(sem_s_max, 1)
                dve.wait_ge(sem_s_max, t + 1)
                nc.vector.tensor_tensor(probs[:, :, :], ps_att[:, :, :], view(s_max[:, :], 0, [[1, Q], [0, H]]),
                                        ALU.subtract).then_inc(sem_s_shifted, 1)

            def transpose_probs(t):
                dve.wait_ge(sem_s_exp, t + 1)
                if t >= 1:
                    dve.wait_ge(sem_context_done, t)
                nc.vector.transpose(eT[:, :, :], probs[:, :, :]).then_inc(sem_eT_ready, 1)

            def residual_2(t):
                dve.wait_ge(sem_context_done, t + 1)
                nc.vector.transpose(oT[:, :, :], view(ps_att[:, 0, :], 0, [[1, H], [H, Q]])).then_inc(sem_oT_ready, 1)
                dve.wait_ge(sem_oT_ready, t + 1)
                nc.vector.reciprocal(o_recip[:, :], oT[:, :, HD]).then_inc(sem_o_recip, 1)
                dve.wait_ge(sem_o_recip, t + 1)
                nc.vector.tensor_tensor(attn[:, :].rearrange("p (h d) -> p h d", d=HD), oT[:, :, 0:HD],
                                        view(o_recip[:, :], 0, [[1, H], [0, HD]]), ALU.mult).then_inc(sem_o_scaled, 1)
                dve.wait_ge(sem_o_scaled, t + 1)
                nc.vector.tensor_tensor(x2[:, t % 2, :], attn[:, :], x1[:, t % 2, :], ALU.add).then_inc(sem_x2_ready, 1)
                dve.wait_ge(sem_x2_ready, t + 1)
                norm_stats(x2[:, t % 2, :], 2, t, sem_ln3_stats, sem_ln3_mean)

            def norm_3(t):
                if t >= 1:
                    dve.wait_ge(sem_h3_transposed, t)
                norm_apply(h3[:, :], x2[:, t % 2, :], 2, t, sem_ln3_rstd, sem_h3_ready)

            def choose_experts(t):
                dve.wait_ge(sem_router_done, t + 1)
                if t >= 1:
                    dve.wait_ge(sem_r_exp, t)
                nc.vector.tensor_copy(r_scores[:, 0, :], ps_t0[:, 2 * P:2 * P + E]).then_inc(sem_r_copied, 1)
                dve.wait_ge(sem_r_copied, t + 1)
                nc.vector.max(r_top[:, 0, :], r_scores[:, 0, :]).then_inc(sem_r_top8, 1)
                dve.wait_ge(sem_r_top8, t + 1)
                nc.vector.match_replace(r_rest[:, :], r_top[:, 0, :], r_scores[:, 0, :], NEG).then_inc(sem_r_first8, 1)
                nc.vector.tensor_scalar(r_negmax[:, :], r_top[:, 0, 0:1], -1.0, None, ALU.mult).then_inc(sem_r_negmax, 1)
                dve.wait_ge(sem_r_first8, t + 1)
                nc.vector.max(r_top[:, 1, :], r_rest[:, :]).then_inc(sem_r_next8, 1)
                dve.wait_ge(sem_r_next8, t + 1)
                nc.vector.match_replace(r_scores[:, 1, :], r_top[:, 1, :], r_rest[:, :], NEG).then_inc(sem_r_masked, 1)

            def gates(t):
                dve.wait_ge(sem_r_exp, t + 1)
                nc.vector.tensor_tensor(gate[:, :], r_exp[:, 0, :], r_exp[:, 1, :], ALU.subtract)\
                    .then_inc(sem_gate_ready, 1)
                dve.wait_ge(sem_gate_ready, t + 1)
                nc.vector.tensor_reduce(gate_sum[:, :], gate[:, :], AX_X, ALU.add).then_inc(sem_gate_sum, 1)
                dve.wait_ge(sem_gate_sum, t + 1)
                nc.vector.reciprocal(gate_recip[:, :], gate_sum[:, :]).then_inc(sem_gate_recip, 1)

            def gate_z(t):
                dve.wait_ge(sem_z_done, t + 1)
                if t >= 1:
                    dve.wait_ge(sem_zg_transposed, t)
                nc.vector.scalar_tensor_tensor(
                    out=zg[:, :].rearrange("p (e r) -> p e r", e=E), in0=ps_b[:, :].rearrange("p (e r) -> p e r", e=E),
                    scalar=SCALING, in1=view(gate[:, :], 0, [[1, E], [0, RANK]]), op0=ALU.mult,
                    op1=ALU.mult).then_inc(sem_z_gated, 1)

            def residual_3(t):
                dve.wait_ge(sem_out_done, t + 1)
                dve.wait_ge(sem_gate_recip, t + 1)
                if t >= 2:
                    dve.wait_ge((sem_y_out0, sem_y_out1)[t % 2], 16 * (t // 2))
                nc.vector.scalar_tensor_tensor(out=y[:, t % 2, :], in0=ps_a[:, :], scalar=gate_recip[:, 0:1],
                                               in1=x2[:, t % 2, :], op0=ALU.mult, op1=ALU.add).then_inc(sem_y_ready, 1)

            scalars()
            dve.wait_ge(sem_x_in, 16)
            for t in range(TILES):
                norm_stats(x_sb[:, t, :], 0, t, sem_ln1_stats, sem_ln1_mean)
            for t in range(TILES):
                if t >= 2:
                    dve.wait_ge(sem_x_u8, t - 1)
                norm_apply(h1[:, t % 2, :], x_sb[:, t, :], 0, t, sem_ln1_rstd, sem_ln1_done)
                if t >= 1:
                    center_q1(t - 1)
                if t >= 2:
                    copy_q1T(t - 2)
            center_q1(TILES - 1)
            copy_q1T(TILES - 2)
            copy_q1T(TILES - 1)
            dve.wait_ge(sem_q1_ready, TILES)
            dve.wait_ge(sem_consts, 4)
            nc.vector.tensor_scalar(row_term[:, :], q1_rowsum[:, :], sc_base[:, 0:1], sc_row[:, 0:1],
                                    ALU.add, ALU.mult).then_inc(sem_row_scale, 1)
            dve.wait_ge(sem_row_scale, 1)
            for t in range(TILES):
                nc.vector.tensor_scalar(x_sb[:, t, :], x_sb[:, t, :], row_term[:, t:t + 1], None,
                                        ALU.add).then_inc(sem_x_shifted, 1)
            dve.wait_ge(sem_x_shifted, TILES)
            for n in range(BPT):
                center_ctx(n)
            finish_product(0)
            residual_1(0)
            norm_2(0)
            for t in range(TILES + 1):
                if t < TILES:
                    q_to_heads(t)
                    k_to_heads(t)
                    center_ctx(BPT * (t + 1))
                    center_ctx(BPT * (t + 1) + 1)
                    v_to_heads(t)
                if t >= 1:
                    choose_experts(t - 1)
                if t < TILES:
                    center_ctx(BPT * (t + 1) + 2)
                    center_ctx(BPT * (t + 1) + 3)
                if t >= 1:
                    gates(t - 1)
                if t < TILES:
                    softmax_shift(t)
                if t >= 1:
                    gate_z(t - 1)
                if t < TILES:
                    transpose_probs(t)
                if t + 1 < TILES:
                    finish_product(t + 1)
                    residual_1(t + 1)
                    norm_2(t + 1)
                if t >= 1:
                    residual_3(t - 1)
                if t < TILES:
                    residual_2(t)
                    norm_3(t)

        @block.tensor
        def _(pe):
            def transpose_q1(t):
                pe.wait_ge(sem_q1_ready, t + 1)
                if t == 0:
                    pe.wait_ge(sem_identity_bf, 1)
                if t >= 2:
                    pe.wait_ge(sem_q1T_ready, t - 1)
                dst = ps_t[t % 2][:, 0:D // 2].bitcast(BF16)
                for c in range(KC):
                    last = nc.tensor.transpose(dst[:, c * P:(c + 1) * P], q1[:, t % 2, c::KC], ident_bf[:, :])
                last.then_inc(sem_q1_transposed, 1)

            def product(t):
                pe.wait_ge(sem_q1T_ready, t + 1)
                if t >= 1:
                    pe.wait_ge(sem_y1_ready, 2 * t)
                for b in range(BPT):
                    n = BPT * t + b
                    pe.wait_ge(sem_ctx_bf, n + 1)
                    for m in range(KC):
                        col = (m % 2) * BPT * LW + b * LW
                        for c in range(KC):
                            last = nc.tensor.matmul(ps1[:, m // 2, col:col + LW],
                                                    cbf[:, n % BF_SLOTS, c, m * P:(m + 1) * P],
                                                    q1T[:, t, c, b, :], start=(c == 0), stop=(c == KC - 1))
                    last.then_inc(sem_stage1_done, 1)

            def transpose_y1(t):
                pe.wait_ge(sem_y1_ready, 2 * (t + 1))
                if t == 0:
                    pe.wait_ge(sem_identity, 1)
                    pe.wait_ge(sem_q1T_ready, TILES)
                if t >= 2:
                    pe.wait_ge(sem_r_copied, t - 1)
                for c in range(KC):
                    last = nc.tensor.transpose(ps_t0[:, c * P:(c + 1) * P], y1T[:, c, :], ident[:, :])
                last.then_inc(sem_y1_transposed, 1)

            def transpose_rows(src, ready, done, t):
                pe.wait_ge(ready, t + 1)
                for c in range(KC):
                    last = nc.tensor.transpose(ps_t1[:, c * P:(c + 1) * P], src[:, c * P:(c + 1) * P], ident[:, :])
                last.then_inc(done, 1)

            def project(dst, aT, w, done):
                for c in range(KC):
                    last = nc.tensor.matmul(dst[:, :], aT[:, c, :], w[:, c, :], start=(c == 0), stop=(c == KC - 1))
                last.then_inc(done, 1)

            def qkv(t):
                pe.wait_ge(sem_h2T_ready, t + 1)
                if t == 0:
                    pe.wait_ge(sem_wq_in, 16)
                if t >= 2:
                    pe.wait_ge(sem_y_ready, t - 1)
                project(ps_a, h2T, wq, sem_q_done)
                if t == 0:
                    pe.wait_ge(sem_wk_in, 16)
                if t >= 2:
                    pe.wait_ge(sem_z_gated, t - 1)
                project(ps_b, h2T, wk, sem_k_done)
                if t >= 1:
                    pe.wait_ge(sem_h2T_ready, t + 1)
                    transpose_rows(h3, sem_h3_ready, sem_h3_transposed, t - 1)
                if t == 0:
                    pe.wait_ge(sem_wv_in, 16)
                pe.wait_ge(sem_q_biased, t + 1)
                project(ps_a, h2T, wv, sem_v_done)

            def router(t):
                pe.wait_ge(sem_h3T_ready, t + 1)
                if t == 0:
                    pe.wait_ge(sem_router_in, 32)
                pe.wait_ge(sem_x1_ready, min(t + 2, TILES))
                if t >= 1:
                    pe.wait_ge(sem_r_copied, t)
                for c in range(KC):
                    last = nc.tensor.matmul(ps_t0[0:RD, 0:P], wr[:, c, :], h3T[:, c, :], start=(c == 0),
                                            stop=(c == KC - 1))
                last.then_inc(sem_router_q_done, 1)
                pe.wait_ge(sem_router_q_ready, t + 1)
                nc.tensor.matmul(ps_t0[:, 2 * P:2 * P + E], router_qT[:, :], keys[:, :], start=True,
                                 stop=True).then_inc(sem_router_done, 1)

            def scores(t):
                pe.wait_ge(sem_q_diag, BPT * (t + 1))
                pe.wait_ge(sem_kT_ready, t + 1)
                if t >= 1:
                    pe.wait_ge(sem_oT_ready, t)
                for i in range(Q):
                    last = nc.tensor.matmul(ps_att[:, i, :], qdiag[:, i, :], kT[:, i, :], start=True, stop=True)
                last.then_inc(sem_scores_done, 1)

            def context(t):
                pe.wait_ge(sem_v_diag, BPT * (t + 1))
                pe.wait_ge(sem_eT_ready, t + 1)
                for i in range(Q):
                    last = nc.tensor.matmul(ps_att[:, i, :], vdiag[:, i, :], eT[:, i, :], start=True, stop=True)
                last.then_inc(sem_context_done, 1)

            def bottleneck(t):
                if t == 0:
                    pe.wait_ge(sem_a_in, 16)
                if t + 1 < TILES:
                    pe.wait_ge(sem_k_biased, t + 2)
                if t == TILES - 1:
                    pe.wait_ge(sem_z_gated, t)
                project(ps_b, h3T, wa, sem_z_done)

            def output(t):
                pe.wait_ge(sem_zgT_ready, t + 1)
                if t == 0:
                    pe.wait_ge(sem_b_in, 16)
                if t + 1 < TILES:
                    pe.wait_ge(sem_v_biased, t + 2)
                if t == TILES - 1:
                    pe.wait_ge(sem_y_ready, t)
                project(ps_a, zgT, wb, sem_out_done)

            for t in range(TILES):
                transpose_q1(t)
            product(0)
            transpose_y1(0)
            transpose_rows(h2, sem_h2_ready, sem_h2_transposed, 0)
            for t in range(TILES + 1):
                if t < TILES:
                    qkv(t)
                else:
                    pe.wait_ge(sem_zgT_ready, t - 1)
                    transpose_rows(h3, sem_h3_ready, sem_h3_transposed, t - 1)
                if t >= 1:
                    router(t - 1)
                if t < TILES:
                    scores(t)
                if t >= 1:
                    bottleneck(t - 1)
                if t + 1 < TILES:
                    product(t + 1)
                if t >= 1:
                    pe.wait_ge(sem_h3T_ready, t)
                    transpose_rows(zg, sem_z_gated, sem_zg_transposed, t - 1)
                if t < TILES:
                    context(t)
                if t + 1 < TILES:
                    transpose_y1(t + 1)
                if t >= 1:
                    output(t - 1)
                if t + 1 < TILES:
                    if t >= 1:
                        pe.wait_ge(sem_zgT_ready, t)
                    else:
                        pe.wait_ge(sem_h2T_ready, 1)
                    transpose_rows(h2, sem_h2_ready, sem_h2_transposed, t + 1)


_INS = [("x", False), ("ctx_4096", False), ("L0_xattn_x1_scale", False), ("L0_xattn_x1_zp", False),
        ("L0_xattn_x2_scale", False), ("L0_xattn_x2_zp", False), ("L0_attn_wq", True), ("L0_attn_bq", False),
        ("L0_attn_wk", True), ("L0_attn_bk", False), ("L0_attn_wv", True), ("L0_attn_bv", False),
        ("L0_ffn_A_w", True), ("L0_ffn_B_w", True), ("L0_ffn_Wq_w", True), ("L0_ffn_keys", True)]


def kernel(**inputs):
    import numpy as _np
    import concourse.bacc as _bacc
    from concourse import mybir as _mybir
    from concourse.bass_utils import run_bass_kernel_spmd as _run

    nc = _bacc.Bacc("TRN2", target_bir_lowering=False, num_devices=1)
    arrays, args = {}, []
    for name, transposed in _INS:
        a = _np.asarray(inputs[name])
        a = _np.ascontiguousarray(a.T if transposed else a)
        arrays[f"in_{name}_dram"] = a
        args.append(nc.dram_tensor(f"in_{name}_dram", a.shape, _mybir.dt.from_np(a.dtype), kind="ExternalInput").ap())
    out = nc.dram_tensor("out_0_dram", inputs["x"].shape, _mybir.dt.float32, kind="ExternalOutput").ap()
    build(nc, *args, out)
    r = _run(nc, [arrays], core_ids=[0])
    return r.results[0]["out_0_dram"]
```
